# Optimizing a Trainium2 kernel written in Bass

```python
import numpy as np
import jax
import jax.numpy as jnp

def _softmax(x, axis=-1):
    return jax.nn.softmax(x, axis=axis)

def _gelu(x):
    return jax.nn.gelu(x, approximate=True)

def _silu(x):
    return jax.nn.silu(x)

def _sigmoid(x):
    return jax.nn.sigmoid(x)

def _layernorm(x, axis=-1, eps=1e-05):
    m = jnp.mean(x, axis=axis, keepdims=True)
    v = jnp.var(x, axis=axis, keepdims=True)
    return (x - m) / jnp.sqrt(v + eps)

def _scatter_add(tgt, idx, src, axis=0):
    return tgt.at[idx].add(src)

def _segment_sum(src, seg, n):
    return jax.ops.segment_sum(src, seg, n)
kernel_name = 'mk_rec_standalone_d1_rec_r8_48d5c0'

def setup_inputs(seed: int=0):
    np.random.seed(seed)
    _w = jnp.asarray

    def _rec_inputs():
        import jax
        import jax.numpy as jnp
        _rk = jax.random.key(seed)
        r_cin_inputs = 7.22013e-05 + 1.00017 * jax.random.normal(jax.random.fold_in(_rk, 1), (512, 32, 64), jnp.float32)
        return r_cin_inputs
    r_cin_inputs = _rec_inputs()

    def _L0_rec_setup():
        import jax, jax.numpy as jnp
        import numpy as np
        FIELD = 32
        DIM = 64
        LAYER_SIZE = (128, 128)

        def _cin(x, weights, biases):
            B, F, D = x.shape
            hidden = x
            finals = []
            n_layers = len(weights)
            for i, (w, b) in enumerate(zip(weights, biases)):
                size = w.shape[0]
                z = jnp.einsum('bhd,bfd->bhfd', hidden, x).reshape(B, hidden.shape[1] * F, D)
                y = jnp.einsum('bcd,oc->bod', z, w) + b[None, :, None]
                y = jax.nn.relu(y)
                if i != n_layers - 1:
                    hidden, direct = (y[:, :size // 2, :], y[:, size // 2:, :])
                else:
                    direct = y
                finals.append(direct)
            return jnp.concatenate(finals, axis=1).sum(-1)
        key = jax.random.key(seed)
        ks = jax.random.split(key, 5)
        B = 512
        x = jax.random.normal(ks[0], (B, FIELD, DIM), dtype=jnp.float32)
        field_nums = [FIELD]
        params = {}
        for i, size in enumerate(LAYER_SIZE):
            in_ch = field_nums[-1] * field_nums[0]
            fan = 1.0 / np.sqrt(in_ch)
            params[f'w{i}'] = jax.random.uniform(ks[1 + 2 * i % 4], (size, in_ch), minval=-fan, maxval=fan, dtype=jnp.float32)
            params[f'b{i}'] = jax.random.uniform(ks[2 + 2 * i % 4], (size,), minval=-fan, maxval=fan, dtype=jnp.float32)
            field_nums.append(size // 2)
        return {'cin_inputs': x, 'w0': params['w0'], 'b0': params['b0'], 'w1': params['w1'], 'b1': params['b1']}
    _L0_rec_all = _L0_rec_setup()
    _L0_rec_in = {k: v for k, v in _L0_rec_all.items() if k in ('w0', 'b0', 'w1', 'b1')}
    del _L0_rec_all
    return {'r_cin_inputs': r_cin_inputs, 'L0_rec_w0': _L0_rec_in['w0'], 'L0_rec_b0': _L0_rec_in['b0'], 'L0_rec_w1': _L0_rec_in['w1'], 'L0_rec_b1': _L0_rec_in['b1']}

def reference(r_cin_inputs, L0_rec_w0, L0_rec_b0, L0_rec_w1, L0_rec_b1):
    import jax
    import jax.numpy as jnp

    def _L0_rec_ref(cin_inputs, w0, b0, w1, b1):
        import jax, jax.numpy as jnp
        import numpy as np
        FIELD = 32
        DIM = 64
        LAYER_SIZE = (128, 128)

        def _cin(x, weights, biases):
            B, F, D = x.shape
            hidden = x
            finals = []
            n_layers = len(weights)
            for i, (w, b) in enumerate(zip(weights, biases)):
                size = w.shape[0]
                z = jnp.einsum('bhd,bfd->bhfd', hidden, x).reshape(B, hidden.shape[1] * F, D)
                y = jnp.einsum('bcd,oc->bod', z, w) + b[None, :, None]
                y = jax.nn.relu(y)
                if i != n_layers - 1:
                    hidden, direct = (y[:, :size // 2, :], y[:, size // 2:, :])
                else:
                    direct = y
                finals.append(direct)
            return jnp.concatenate(finals, axis=1).sum(-1)
        return _cin(cin_inputs, [w0, w1], [b0, b1])
    y = _L0_rec_ref(r_cin_inputs, L0_rec_w0, L0_rec_b0, L0_rec_w1, L0_rec_b1)
    return y

_drawn_inputs = setup_inputs


def setup_inputs(seed=0):
    import zlib

    import numpy as np

    out = dict(_drawn_inputs(seed))
    spreads = {}
    factors = {}
    for name, (base, spread) in spreads.items():
        noise = np.random.default_rng([zlib.crc32(name.encode()), seed]).standard_normal(out[name].shape)
        drawn = base * np.exp(spread * noise) if base else spread * noise
        out[name] = jnp.asarray(drawn.astype(out[name].dtype))
    for name, factor in factors.items():
        out[name] = (out[name] * factor).astype(out[name].dtype)
    return out
```

```python
from contextlib import ExitStack

import concourse.bass as bass
from concourse import mybir

F32 = mybir.dt.float32
F32R = mybir.dt.float32r
ALU = mybir.AluOpType
ACT = mybir.ActivationFunctionType
AX_X = mybir.AxisListType.X

P = 128
F = 32
HID = 64
C = 1024
BANK = 512
KK = P // F
SLOTS = 10
L0_SLOTS = (0, 2)
L1_SLOTS = tuple(r for r in range(SLOTS) if r not in L0_SLOTS)
NATIVE = (5, 9)
LOW_DVE = (7,)
Z_RING, HL_RING, XB_RING = 5, 4, 2
LEAD = 4
REST_SLOT, XSPLIT_SLOT, RELU1_SLOT, SUM1_SLOT, RELU0_SLOT, SUM0_SLOT = 2, 3, 4, 5, 7, 8


def cin_kernel(nc: bass.Bass, x_rows, w0_fwd, w0_bwd, w1_tiles, b0, b1, out):
    N = x_rows.shape[1]
    D = 64
    NB = N // C
    SB = C // D
    LAST = NB - 1
    NC = C // BANK

    def exists(b, r):
        return 0 <= b <= LAST if r in L1_SLOTS else -1 <= b < LAST

    order = [(b, r) for b in range(-1, NB) for r in range(SLOTS) if exists(b, r)]
    kinds = {
        "all": lambda r: True,
        "cross": lambda r: r in L1_SLOTS,
        "split": lambda r: r not in NATIVE,
        "low_dve": lambda r: r not in NATIVE and r in LOW_DVE,
        "low_pool": lambda r: r not in NATIVE and r not in LOW_DVE,
    }
    per_block = {k: sum(f(r) for r in range(SLOTS)) for k, f in kinds.items()}
    upto = {k: {} for k in kinds}
    for k, f in kinds.items():
        n = 0
        for b, r in order:
            n += f(r)
            upto[k][b, r] = n
    units_of = {k: [u for u in order if f(u[1])] for k, f in kinds.items()}
    assert 2 * per_block["all"] % Z_RING == 0 and 2 * per_block["split"] % HL_RING == 0

    ctx = ExitStack()
    with ctx:
        def sb(name, shape, dt=F32):
            return ctx.enter_context(nc.sbuf_tensor(name, shape, dt))

        def sem(name):
            return ctx.enter_context(nc.semaphore(name))

        w1n = sb("w1n", [P, 2 * len(NATIVE), P])
        w1h = sb("w1h", [P, 16, P], F32R)
        w1l = sb("w1l", [P, 16, P], F32R)
        w0h = sb("w0h", [P, 4, P], F32R)
        w0l = sb("w0l", [P, 4, P], F32R)
        wr = sb("wr", [P, P], F32R)
        pick = sb("pick", [P, 8, P], F32R)
        bias0 = sb("bias0", [P, 1])
        bias1 = sb("bias1", [P, 1])
        x4 = sb("x4", [P, 2, C])
        rot = sb("rot", [P, 2, 2, C])
        rot16 = sb("rot16", [P, C])
        xs = sb("xs", [P, 2, C], F32R)
        z = sb("z", [P, Z_RING, 2, C])
        zh = sb("zh", [P, HL_RING, 2, C], F32R)
        zl = sb("zl", [P, HL_RING, 2, C], F32R)
        zr = sb("zr", [P, C])
        zrs = sb("zrs", [P, C], F32R)
        y0r = sb("y0r", [P, C])
        y1r = sb("y1r", [P, C])
        hid4 = sb("hid4", [P, 2, 2, C])
        sums0 = sb("sums0", [P, N // D])
        sums1 = sb("sums1", [P, N // D])

        y0 = ctx.enter_context(nc.psum_tensor("y0", [P, C], F32))
        y1 = ctx.enter_context(nc.psum_tensor("y1", [P, C], F32))
        xb = ctx.enter_context(nc.psum_tensor("xb", [P, XB_RING, C], F32))

        w0a = z[:, 0, 0, 0:512].rearrange("p (j o) -> p j o", j=4)
        w0b = z[:, 0, 0, 512:1024].rearrange("p (j o) -> p j o", j=4)
        w0s = z[:, 0, 1, 0:512].rearrange("p (j o) -> p j o", j=4)
        ra, rb, rs = z[:, 1, 0, 0:128], z[:, 1, 0, 128:256], z[:, 1, 0, 256:384]
        picks = z[:, 2, 0, :]
        w1 = z[:, 3].rearrange("p a (t o) -> p (a t) o", o=P)
        rl = sb("rl", [P, P], F32R)

        s_w0_in, s_wr_in, s_w1_in, s_b_in = sem("s_w0_in"), sem("s_wr_in"), sem("s_w1_in"), sem("s_b_in")
        s_w0_zero, s_wr_zero = sem("s_w0_zero"), sem("s_wr_zero")
        s_w0_sum, s_w0_high, s_w0_low = sem("s_w0_sum"), sem("s_w0_high"), sem("s_w0_low")
        s_wr_sum, s_wr_high, s_wr_low, s_wr_put = sem("s_wr_sum"), sem("s_wr_high"), sem("s_wr_low"), sem("s_wr_put")
        s_w1_high, s_w1_low = sem("s_w1_high"), sem("s_w1_low")
        s_pick0, s_pick1, s_pick = sem("s_pick0"), sem("s_pick1"), sem("s_pick")
        s_x4_in = [sem("s_x4_in0"), sem("s_x4_in1")]
        s_rot_in = [sem("s_rot_in0"), sem("s_rot_in1")]
        s_rot16_in = sem("s_rot16_in")
        s_hid_in = [sem("s_hid_in0"), sem("s_hid_in1")]
        s_xhigh, s_xsplit = sem("s_xhigh"), sem("s_xsplit")
        s_xb = sem("s_xb")
        s_mult = sem("s_mult")
        s_high = sem("s_high")
        s_low_dve, s_low_pool = sem("s_low_dve"), sem("s_low_pool")
        s_used = sem("s_used")
        s_rest_mult, s_rest_high, s_rest_low, s_rest_used = (
            sem("s_rest_mult"), sem("s_rest_high"), sem("s_rest_low"), sem("s_rest_used"))
        s_relu0, s_relu1, s_sum0, s_sum1 = sem("s_relu0"), sem("s_relu1"), sem("s_sum0"), sem("s_sum1")
        s_out = sem("s_out")

        def blocks(eng, iteration):
            for b in (-1, 0, 1):
                iteration(b, 0)
            with eng.Fori(0, (NB - 4) // 2) as pair:
                iteration(2, pair * 2)
                iteration(3, pair * 2)
            for b in (LAST - 1, LAST):
                iteration(b, 0)

        def count(kind, u, past):
            return upto[kind][u] + per_block[kind] * past

        def wait_unit(eng, s, kind, u, past):
            eng.wait_ge(s, count(kind, u, past))

        def back(kind, u, n):
            i = upto[kind][u] - 1 - n
            return units_of[kind][i] if i >= 0 else None

        def slot_of(kind, u, ring):
            return (upto[kind][u] - 1) % ring

        def wait_low(eng, u, past):
            if u[1] in LOW_DVE:
                wait_unit(eng, s_low_dve, "low_dve", u, past)
            else:
                wait_unit(eng, s_low_pool, "low_pool", u, past)

        block = ctx.enter_context(nc.Block())

        @block.sync
        def _(sp):
            def load(n, past):
                cols = bass.ds(n * C + C * past, C)
                if n >= 1:
                    sp.wait_ge(s_rest_mult, n + past)
                for g in range(KK):
                    sp.dma_start(rot16[g * F:(g + 1) * F, :], x_rows[16:16 + F, cols]).then_inc(s_rot16_in, 16)
                for q in range(2):
                    for g in range(KK):
                        rows = bass.AP(x_rows.tensor, x_rows.offset + g * N, [[N, F], [KK * N, 4], [1, N]])
                        sp.dma_start(rot[g * F:(g + 1) * F, q, :, :],
                                     rows[:, 2 * q:2 * q + 2, cols]).then_inc(s_rot_in[q], 16)
                if n >= 2:
                    sp.wait_ge(s_xsplit, n - 1 + past)
                for g in range(KK):
                    sp.dma_start(x4[g * F:(g + 1) * F, n % 2, :], x_rows[0:F, cols]).then_inc(s_x4_in[n % 2], 16)

            def copy_hidden(n, past):
                sp.wait_ge(s_relu0, n + 1 + past)
                for half in range(2):
                    for g in range(KK):
                        sp.dma_start(hid4[g * F:(g + 1) * F, n % 2, half, :],
                                     y0r[half * F:(half + 1) * F, :]).then_inc(s_hid_in[n % 2], 16)

            sp.dma_start(w0a, w0_fwd[0:512, :].rearrange("(j p) o -> p j o", p=P)).then_inc(s_w0_in, 16)
            sp.wait_ge(s_w0_zero, 1)
            sp.dma_start(w0b[:, 1:4, :], w0_bwd[128:512, :].rearrange("(j p) o -> p j o", p=P)).then_inc(s_w0_in, 16)
            sp.dma_start(w0b[F:P, 0, :], w0_bwd[F:P, :]).then_inc(s_w0_in, 16)
            load(0, 0)
            for g in range(2):
                sp.dma_start(ra[g * F:(g + 1) * F, :], w0_fwd[512:544, :]).then_inc(s_wr_in, 16)
                sp.dma_start(rb[g * F:(g + 1) * F, :], w0_bwd[512:544, :]).then_inc(s_wr_in, 16)
            sp.dma_start(bias0[:, :], b0).then_inc(s_b_in, 16)
            sp.dma_start(bias1[:, :], b1).then_inc(s_b_in, 16)
            sp.dma_start(w1, w1_tiles.rearrange("p (t o) -> p t o", o=P)).then_inc(s_w1_in, 16)
            sp.wait_ge(s_wr_high, 1)
            sp.wait_ge(s_wr_low, 1)
            for g in range(2):
                rows = slice(F * g + 16, F * g + 32)
                sp.dma_start(wr[rows, :].bitcast(F32), rl[rows, :].bitcast(F32)).then_inc(s_wr_put, 16)

            def iteration(b, past):
                if b + 2 <= LAST:
                    load(b + 2, past)
                if b + 1 <= LAST:
                    copy_hidden(b + 1, past)

            blocks(sp, iteration)
            sp.wait_ge(s_sum0, NB)
            sp.dma_start(out[0:HID, :], sums0[HID:P, :]).then_inc(s_out, 16)
            sp.wait_ge(s_sum1, NB)
            sp.dma_start(out[HID:HID + P, :], sums1[:, :]).then_inc(s_out, 16)
            sp.wait_ge(s_out, 32)

        @block.gpsimd
        def _(pool):
            nc.gpsimd.memset(picks, 0.0).then_inc(s_pick0, 1)
            pool.wait_ge(s_pick0, 1)
            for part in range(2):
                v = picks[part * F:(part + 1) * F, :].rearrange("p (t g h) -> p t g h", t=8, g=KK)
                nc.gpsimd.affine_select(out=v, in_=v, compare_op=ALU.not_equal, fill=1.0, base=0,
                                        pattern=[[-KK, 8], [-1, KK], [0, F]],
                                        channel_multiplier=1).then_inc(s_pick1, 1)

            def iteration(b, past):
                for r in range(SLOTS):
                    u = (b, r)
                    if exists(*u) and r not in NATIVE and r not in LOW_DVE:
                        wait_unit(pool, s_high, "split", u, past)
                        s = slot_of("split", u, HL_RING)
                        nc.gpsimd.tensor_tensor(zl[:, s], z[:, slot_of("all", u, Z_RING)], zh[:, s],
                                                ALU.subtract).then_inc(s_low_pool, 1)

            blocks(pool, iteration)

        @block.scalar
        def _(act):
            act.wait_ge(s_w0_sum, 1)
            nc.scalar.activation(w0h[:, :, :], w0s, ACT.Copy).then_inc(s_w0_high, 1)
            act.wait_ge(s_pick1, 2)
            nc.scalar.activation(pick[:, :, :].rearrange("p t o -> p (t o)"), picks, ACT.Copy).then_inc(s_pick, 1)
            act.wait_ge(s_wr_sum, 1)
            act.wait_ge(s_wr_zero, 1)
            nc.scalar.activation(wr[0:2 * F, :], rs[0:2 * F, :], ACT.Copy).then_inc(s_wr_high, 1)
            act.wait_ge(s_w1_in, 16)
            nc.scalar.activation(w1h[:, :, :], w1, ACT.Copy).then_inc(s_w1_high, 1)
            act.wait_ge(s_b_in, 32)

            def relu1(b, past):
                wait_unit(act, s_used, "all", (b, SLOTS - 1), past)
                if b >= 1:
                    act.wait_ge(s_sum1, b + past)
                nc.scalar.activation(y1r[:, :], y1[:, :], ACT.Relu, bias=bias1[:, :]).then_inc(s_relu1, 1)

            def iteration(b, past):
                n = b + 1
                for r in range(SLOTS):
                    u = (b, r)
                    if exists(*u) and r not in NATIVE:
                        wait_unit(act, s_mult, "all", u, past)
                        free = back("split", u, HL_RING)
                        if free:
                            wait_unit(act, s_used, "all", free, past)
                        nc.scalar.activation(zh[:, slot_of("split", u, HL_RING)], z[:, slot_of("all", u, Z_RING)],
                                             ACT.Copy).then_inc(s_high, 1)
                    if r == REST_SLOT and n <= LAST:
                        act.wait_ge(s_rest_mult, n + 1 + past)
                        if n >= 1:
                            act.wait_ge(s_rest_used, n + past)
                        nc.scalar.activation(zrs[:, :], zr[:, :], ACT.Copy).then_inc(s_rest_high, 1)
                    if r == XSPLIT_SLOT and n <= LAST:
                        act.wait_ge(s_x4_in[n % 2], 64 * (n // 2 + 1) + 32 * past)
                        if n >= 2:
                            wait_unit(act, s_xb, "cross", (n - 2, SLOTS - 1), past)
                        nc.scalar.activation(xs[:, n % 2, :], x4[:, n % 2, :], ACT.Copy).then_inc(s_xhigh, 1)
                    if r == RELU1_SLOT and b >= 1:
                        relu1(b - 1, past)
                    if r == RELU0_SLOT and n <= LAST:
                        act.wait_ge(s_rest_used, n + 1 + past)
                        if n >= 1:
                            m = n - 1
                            act.wait_ge(s_hid_in[m % 2], 128 * (m // 2 + 1) + 64 * past)
                            act.wait_ge(s_sum0, n + past)
                        nc.scalar.activation(y0r[:, :], y0[:, :], ACT.Relu, bias=bias0[:, :]).then_inc(s_relu0, 1)

            blocks(act, iteration)
            relu1(LAST, 0)

        @block.vector
        def _(dve):
            nc.vector.memset(w0b[:, 0, :], 0.0).then_inc(s_w0_zero, 1)
            nc.vector.memset(wr[:, :].bitcast(F32), 0.0).then_inc(s_wr_zero, 1)
            dve.wait_ge(s_w0_in, 48)
            nc.vector.tensor_tensor(w0s, w0a, w0b, ALU.add).then_inc(s_w0_sum, 1)
            dve.wait_ge(s_w0_high, 1)
            nc.vector.tensor_tensor(w0l[:, :, :], w0s, w0h[:, :, :], ALU.subtract).then_inc(s_w0_low, 1)
            dve.wait_ge(s_wr_in, 64)
            nc.vector.tensor_tensor(rs[0:2 * F, :], ra[0:2 * F, :], rb[0:2 * F, :], ALU.add).then_inc(s_wr_sum, 1)
            dve.wait_ge(s_wr_high, 1)
            nc.vector.tensor_tensor(rl[0:2 * F, :], rs[0:2 * F, :], wr[0:2 * F, :], ALU.subtract).then_inc(s_wr_low, 1)
            dve.wait_ge(s_w0_low, 1)
            dve.wait_ge(s_wr_low, 1)
            dve.wait_ge(s_pick, 1)

            def low(u, past):
                wait_unit(dve, s_high, "split", u, past)
                s = slot_of("split", u, HL_RING)
                nc.vector.tensor_tensor(zl[:, s], z[:, slot_of("all", u, Z_RING)], zh[:, s],
                                        ALU.subtract).then_inc(s_low_dve, 1)

            def sum1(b, past):
                dve.wait_ge(s_relu1, b + 1 + past)
                nc.vector.tensor_reduce(sums1[:, bass.ds(b * SB + SB * past, SB)],
                                        y1r[:, :].rearrange("p (s d) -> p s d", d=D), AX_X,
                                        ALU.add).then_inc(s_sum1, 1)

            def iteration(b, past):
                n = b + 1
                for r in range(SLOTS):
                    u = (b, r)
                    if exists(*u):
                        free = back("all", u, Z_RING)
                        if free and free[1] in NATIVE:
                            wait_unit(dve, s_used, "all", free, past)
                        elif free:
                            wait_low(dve, free, past)
                        zu = z[:, slot_of("all", u, Z_RING)]
                        if r in L0_SLOTS:
                            q = L0_SLOTS.index(r)
                            dve.wait_ge(s_x4_in[n % 2], 64 * (n // 2 + 1) + 32 * past)
                            dve.wait_ge(s_rot_in[q], 64 * (n + 1) + 64 * past)
                            nc.vector.tensor_tensor(zu, x4[:, n % 2, :].unsqueeze(1).broadcast_to([P, 2, C]),
                                                    rot[:, q], ALU.mult).then_inc(s_mult, 1)
                        else:
                            if r == L1_SLOTS[0]:
                                dve.wait_ge(s_hid_in[b % 2], 128 * (b // 2 + 1) + 64 * past)
                            wait_unit(dve, s_xb, "cross", u, past)
                            xbu = xb[:, slot_of("cross", u, XB_RING), :]
                            nc.vector.tensor_tensor(zu, xbu.unsqueeze(1).broadcast_to([P, 2, C]), hid4[:, b % 2],
                                                    ALU.mult).then_inc(s_mult, 1)
                    if r == REST_SLOT and n <= LAST:
                        dve.wait_ge(s_x4_in[n % 2], 64 * (n // 2 + 1) + 32 * past)
                        dve.wait_ge(s_rot16_in, 64 * (n + 1) + 64 * past)
                        if n >= 1:
                            dve.wait_ge(s_rest_low, n + past)
                        nc.vector.tensor_tensor(zr[:, :], x4[:, n % 2, :], rot16[:, :], ALU.mult).then_inc(s_rest_mult, 1)
                    if r - 1 in LOW_DVE and exists(b, r - 1):
                        low((b, r - 1), past)
                    if r == REST_SLOT + 1 and n <= LAST:
                        dve.wait_ge(s_rest_high, n + 1 + past)
                        nc.vector.tensor_tensor(zrs[F:2 * F, :], zr[F:2 * F, :], zrs[F:2 * F, :],
                                                ALU.subtract).then_inc(s_rest_low, 1)
                    if r == XSPLIT_SLOT + 1 and n <= LAST:
                        dve.wait_ge(s_xhigh, n + 1 + past)
                        nc.vector.tensor_tensor(xs[F:2 * F, n % 2, :], x4[F:2 * F, n % 2, :], xs[F:2 * F, n % 2, :],
                                                ALU.subtract).then_inc(s_xsplit, 1)
                    if r == SUM1_SLOT and b >= 1:
                        sum1(b - 1, past)
                    if r == SUM0_SLOT and n <= LAST:
                        dve.wait_ge(s_relu0, n + 1 + past)
                        nc.vector.tensor_reduce(sums0[HID:P, bass.ds(n * SB + SB * past, SB)],
                                                y0r[HID:P, :].rearrange("p (s d) -> p s d", d=D), AX_X,
                                                ALU.add).then_inc(s_sum0, 1)
                    if b == -1 and r == L0_SLOTS[1]:
                        dve.wait_ge(s_w1_high, 1)
                        for k, native in enumerate(NATIVE):
                            t = L1_SLOTS.index(native)
                            nc.vector.tensor_copy(w1n[:, 2 * k:2 * k + 2, :], w1[:, 2 * t:2 * t + 2, :]).then_inc(s_w1_low, 1)
                        nc.vector.tensor_tensor(w1l[:, :, :], w1, w1h[:, :, :],
                                                ALU.subtract).then_inc(s_w1_low, 1)
                        dve.wait_ge(s_w1_low, 1 + len(NATIVE))

            blocks(dve, iteration)
            sum1(LAST, 0)

        @block.tensor
        def _(pe):
            pe.wait_ge(s_w0_low, 1)
            pe.wait_ge(s_w0_high, 1)
            pe.wait_ge(s_pick, 1)

            def broadcast_x(u, past):
                b, r = u
                t = L1_SLOTS.index(r)
                if t == 0:
                    pe.wait_ge(s_xsplit, b + 1 + past)
                free = back("cross", u, XB_RING)
                if free:
                    wait_unit(pe, s_mult, "all", free, past)
                for c in range(NC):
                    last = nc.tensor.matmul(xb[:, slot_of("cross", u, XB_RING), c * BANK:(c + 1) * BANK],
                                            pick[:, t, :], xs[:, b % 2, c * BANK:(c + 1) * BANK],
                                            start=True, stop=True)
                last.then_inc(s_xb, 1)

            def contract(u, past):
                b, r = u
                if r in L0_SLOTS:
                    q = L0_SLOTS.index(r)
                    y, wh, wl, w, first, final = y0, w0h, w0l, None, q == 0, False
                    tiles = (2 * q, 2 * q + 1)
                    if first and b >= 0:
                        pe.wait_ge(s_relu0, b + 1 + past)
                else:
                    t = L1_SLOTS.index(r)
                    y, wh, wl, w, first, final = y1, w1h, w1l, w1n, t == 0, t == 7
                    tiles = (2 * t, 2 * t + 1)
                    if first and b >= 1:
                        pe.wait_ge(s_relu1, b + past)
                    if first and b == 0:
                        pe.wait_ge(s_w1_high, 1)
                        pe.wait_ge(s_w1_low, 1 + len(NATIVE))
                zs = slot_of("all", u, Z_RING)
                if r in NATIVE:
                    wait_unit(pe, s_mult, "all", u, past)
                    at = 2 * NATIVE.index(r)
                    terms = [(w[:, at + k, :], z[:, zs, k]) for k in range(2)]
                    groups = [terms]
                else:
                    wait_unit(pe, s_high, "split", u, past)
                    s = slot_of("split", u, HL_RING)
                    groups = [[(ww[:, tile, :], zh[:, s, k]) for k, tile in enumerate(tiles) for ww in (wh, wl)],
                              [(wh[:, tile, :], zl[:, s, k]) for k, tile in enumerate(tiles)]]
                for n_group, group in enumerate(groups):
                    if n_group == 1:
                        wait_low(pe, u, past)
                    for n_term, (weights, moving) in enumerate(group):
                        for c in range(NC):
                            last = nc.tensor.matmul(
                                y[:, c * BANK:(c + 1) * BANK], weights, moving[:, c * BANK:(c + 1) * BANK],
                                start=first and n_group == 0 and n_term == 0,
                                stop=final and n_group == len(groups) - 1 and n_term == len(group) - 1)
                last.then_inc(s_used, 1)

            def iteration(b, past):
                n = b + 1
                for r in range(SLOTS):
                    ahead = (b + (r + LEAD) // SLOTS, (r + LEAD) % SLOTS)
                    if ahead[1] in L1_SLOTS and exists(*ahead):
                        broadcast_x(ahead, past)
                    if exists(b, r):
                        contract((b, r), past)
                    if r == REST_SLOT and n <= LAST:
                        if n == 0:
                            pe.wait_ge(s_wr_put, 32)
                            pe.wait_ge(s_wr_high, 1)
                        pe.wait_ge(s_rest_low, n + 1 + past)
                        for c in range(NC):
                            last = nc.tensor.matmul(y0[:, c * BANK:(c + 1) * BANK], wr[:, :],
                                                    zrs[:, c * BANK:(c + 1) * BANK], start=False, stop=True)
                        last.then_inc(s_rest_used, 1)

            blocks(pe, iteration)


def kernel(r_cin_inputs, L0_rec_w0, L0_rec_b0, L0_rec_w1, L0_rec_b1):
    import numpy as np
    import concourse.bacc as bacc
    from concourse.bass_utils import run_bass_kernel_spmd

    x = np.asarray(r_cin_inputs)
    B, F_, D = x.shape
    x = x.transpose(1, 0, 2).reshape(F_, B * D)
    x_rows = np.ascontiguousarray(np.concatenate([x, x[:16]], axis=0))
    w0 = np.asarray(L0_rec_w0).T.reshape(F_, F_, -1)
    i = np.arange(F_)
    near = np.stack([w0[i, (i + k) % F_] for k in range(17)]).reshape(17 * F_, -1)
    far = np.stack([w0[(i + k) % F_, i] for k in range(17)]).reshape(17 * F_, -1)
    w1 = np.asarray(L0_rec_w1).T.reshape(2, 32, 8, 4, -1).transpose(3, 1, 2, 0, 4).reshape(128, -1)
    arrays = {
        "x_rows": x_rows,
        "w0_fwd": np.ascontiguousarray(near),
        "w0_bwd": np.ascontiguousarray(far),
        "w1_tiles": np.ascontiguousarray(w1),
        "b0": np.ascontiguousarray(np.asarray(L0_rec_b0).reshape(-1, 1)),
        "b1": np.ascontiguousarray(np.asarray(L0_rec_b1).reshape(-1, 1)),
    }
    nc = bacc.Bacc("TRN2", target_bir_lowering=False, num_devices=1)
    args = [nc.dram_tensor(name, a.shape, mybir.dt.from_np(a.dtype), kind="ExternalInput").ap()
            for name, a in arrays.items()]
    args.append(nc.dram_tensor("out", (192, B), F32, kind="ExternalOutput").ap())
    cin_kernel(nc, *args)
    r = run_bass_kernel_spmd(nc, [arrays], core_ids=[0])
    return np.ascontiguousarray(r.results[0]["out"].T)
```

```python
from contextlib import ExitStack

import concourse.bass as bass
from concourse import mybir

F32 = mybir.dt.float32
F32R = mybir.dt.float32r
ALU = mybir.AluOpType
ACT = mybir.ActivationFunctionType
AX_X = mybir.AxisListType.X

P = 128
F = 32
HID = 64
D = 64
C = 512
KK = P // F
UNITS = 4
AHEAD = 2
A_SPLIT = (2,)
A_NATIVE = tuple(v for v in range(UNITS) if v not in A_SPLIT)
L0_AFTER = 2
XB_AT = ((0, 0), (0, 0), (1, 1), (3, 0))
XB_LEAD = 3
HEAD = 6
BODY = 6
DVE_STEPS = {'sum1': 2, 'sum0': 1}
ACT_STEPS = {'square_high': 1, 'rest_high': 2, 'x_high': 0, 'relu1': 1, 'relu0': 0}
POOL_ORDER = ('square', 'rest', 'square_low', 'low_a', 'rest_low', 'x_low')
XB_RING, Z_RING, B_RING, A_RING, SQ_RING, HID_RING, XS_RING = 3, 6, 6, 2, 2, 3, 3


def cin_kernel(nc: bass.Bass, x_rows, w0_near, w0_far, w1_tiles, b0, b1, out):
    N = x_rows.shape[1]
    NB = N // C
    SB = C // D
    LAST = NB - 1

    def unit(b, v):
        return UNITS * b + v

    def units_done(b, v, past):
        return unit(b, v) + 1 + UNITS * past

    def a_splits_done(b, v, past):
        return len(A_SPLIT) * b + sum(s <= v for s in A_SPLIT) + len(A_SPLIT) * past

    assert BODY * len(A_SPLIT) % A_RING == BODY % SQ_RING == BODY % HID_RING == BODY % XS_RING == BODY % 2 == 0
    assert all(BODY * UNITS % ring == 0 for ring in (Z_RING, B_RING, XB_RING))

    ctx = ExitStack()
    with ctx:
        def sb(name, shape, dt=F32):
            return ctx.enter_context(nc.sbuf_tensor(name, shape, dt))

        def sem(name):
            return ctx.enter_context(nc.semaphore(name))

        N_SPLIT = UNITS + len(A_SPLIT)
        w0h, w0l = sb("w0h", [P, 4, P], F32R), sb("w0l", [P, 4, P], F32R)
        w1h, w1l = sb("w1h", [P, N_SPLIT, 2, P], F32R), sb("w1l", [P, N_SPLIT, 2, P], F32R)
        w1n = sb("w1n", [P, len(A_NATIVE), 2, P])
        wr, wr_low = sb("wr", [P, P], F32R), sb("wr_low", [P, P], F32R)
        pick = sb("pick", [P, 8, P], F32R)
        bias0, bias1 = sb("bias0", [P, 1]), sb("bias1", [P, 1])
        x4 = sb("x4", [P, 2, C])
        rot = sb("rot", [P, 2, 4, C])
        rot16 = sb("rot16", [P, 2, C])
        xs = sb("xs", [P, XS_RING, C], F32R)
        sqh, sql = sb("sqh", [P, SQ_RING, 4, C], F32R), sb("sql", [P, SQ_RING, 4, C], F32R)
        zr, zrs = sb("zr", [P, C]), sb("zrs", [P, C], F32R)
        za = sb("za", [P, Z_RING, 2, C])
        bh, bl = sb("bh", [P, B_RING, 2, C], F32R), sb("bl", [P, B_RING, 2, C], F32R)
        ah, al = sb("ah", [P, A_RING, 2, C], F32R), sb("al", [P, A_RING, 2, C], F32R)
        y0r, y1r = sb("y0r", [P, C]), sb("y1r", [P, C])
        hid4 = sb("hid4", [P, HID_RING, 2, C])
        sums0, sums1 = sb("sums0", [P, N // D]), sb("sums1", [P, N // D])

        y0 = ctx.enter_context(nc.psum_tensor("y0", [P, C], F32))
        y1 = ctx.enter_context(nc.psum_tensor("y1", [P, C], F32))
        xb = ctx.enter_context(nc.psum_tensor("xb", [P, XB_RING, 2, C], F32))

        w1raw = za[:, 0:2].rearrange("p r k (c o) -> p (r k c) o", o=P).rearrange(
            "p (v h k) o -> p v h k o", h=2, k=2)
        w0a = za[:, 2, 0, :].rearrange("p (j o) -> p j o", j=4)
        w0b = za[:, 2, 1, :].rearrange("p (j o) -> p j o", j=4)
        w0s = za[:, 3, 0, :].rearrange("p (j o) -> p j o", j=4)
        ra, rb, rs = za[:, 3, 1, 0:P], za[:, 3, 1, P:2 * P], za[:, 3, 1, 2 * P:3 * P]
        picks = hid4[:, HID_RING - 1].rearrange("p h c -> p (h c)")

        s_w0_in, s_wr_in, s_w1_in, s_b_in = sem("s_w0_in"), sem("s_wr_in"), sem("s_w1_in"), sem("s_b_in")
        s_zeros, s_rot16_zero = sem("s_zeros"), sem("s_rot16_zero")
        s_w0_sum, s_w0_high, s_w0_low = sem("s_w0_sum"), sem("s_w0_high"), sem("s_w0_low")
        s_wr_sum, s_wr_high, s_wr_low, s_wr_put = sem("s_wr_sum"), sem("s_wr_high"), sem("s_wr_low"), sem("s_wr_put")
        s_w1_high, s_w1_low, s_w1_whole = sem("s_w1_high"), sem("s_w1_low"), sem("s_w1_whole")
        s_pick0, s_pick1, s_pick = sem("s_pick0"), sem("s_pick1"), sem("s_pick")
        s_x4_in = [sem("s_x4_in0"), sem("s_x4_in1")]
        s_rot_in = [sem("s_rot_in0"), sem("s_rot_in1")]
        s_rot16_in = [sem("s_rot16_in0"), sem("s_rot16_in1")]
        s_hid_in = [sem("s_hid_in0"), sem("s_hid_in1")]
        s_x_high, s_x_low = sem("s_x_high"), sem("s_x_low")
        s_square, s_square_high, s_square_low = sem("s_square"), sem("s_square_high"), sem("s_square_low")
        s_square_used, s_rest_used = sem("s_square_used"), sem("s_rest_used")
        s_rest, s_rest_high, s_rest_low = sem("s_rest"), sem("s_rest_high"), sem("s_rest_low")
        s_xb, s_unit_used = sem("s_xb"), sem("s_unit_used")
        s_a, s_b, s_b_high, s_b_low = sem("s_a"), sem("s_b"), sem("s_b_high"), sem("s_b_low")
        s_a_high, s_a_low = sem("s_a_high"), sem("s_a_low")
        s_relu0, s_relu1, s_sum0, s_sum1 = sem("s_relu0"), sem("s_relu1"), sem("s_sum0"), sem("s_sum1")
        s_out = sem("s_out")

        def blocks(eng, iteration):
            first = HEAD - AHEAD
            trips = (NB - AHEAD - 2 - first) // BODY
            for b in range(-AHEAD, first):
                iteration(b, 0)
            with eng.Fori(0, trips) as trip:
                for b in range(first, first + BODY):
                    iteration(b, trip * BODY)
            for b in range(first + BODY * trips, NB):
                iteration(b, 0)

        def place(b, v):
            return unit(b, v) % XB_RING

        def xb_of(b, v):
            return xb[:, place(b, v)]

        def landed(dmas, n, past):
            return 16 * dmas * (n // 2 + 1) + 8 * dmas * past

        block = ctx.enter_context(nc.Block())

        @block.sync
        def _(sp):
            def load(n, past):
                cols = bass.ds(n * C + C * past, C)
                if n >= 2:
                    sp.wait_ge(s_square_used, n - 1 + past)
                for g in range(KK):
                    rows = bass.AP(x_rows.tensor, x_rows.offset + g * N, [[N, F], [KK * N, 4], [1, N]])
                    sp.dma_start(rot[g * F:(g + 1) * F, n % 2, :, :], rows[:, :, cols]).then_inc(s_rot_in[n % 2], 16)
                if n >= 2:
                    sp.wait_ge(s_x_low, n - 1 + past)
                for g in range(KK):
                    sp.dma_start(x4[g * F:(g + 1) * F, n % 2, :], x_rows[0:F, cols]).then_inc(s_x4_in[n % 2], 16)
                if n >= 2:
                    sp.wait_ge(s_rest, n - 1 + past)
                for g in range(2):
                    sp.dma_start(rot16[g * F:(g + 1) * F, n % 2, :],
                                 x_rows[16:16 + F, cols]).then_inc(s_rot16_in[n % 2], 16)

            def copy_hidden(n, past):
                sp.wait_ge(s_relu0, n + 1 + past)
                for g in range(KK):
                    for half in range(2):
                        sp.dma_start(hid4[g * F:(g + 1) * F, n % HID_RING, half, :],
                                     y0r[half * F:(half + 1) * F, :]).then_inc(s_hid_in[n % 2], 16)

            load(0, 0)
            load(1, 0)
            sp.wait_ge(s_wr_high, 1)
            sp.wait_ge(s_wr_low, 1)
            for g in range(2):
                rows = slice(F * g + 16, F * g + 32)
                sp.dma_start(wr[rows, :].bitcast(F32), wr_low[rows, :].bitcast(F32)).then_inc(s_wr_put, 16)

            def iteration(b, past):
                n = b + AHEAD
                if n <= LAST:
                    copy_hidden(n, past)
                if n + 2 <= LAST:
                    load(n + 2, past)

            blocks(sp, iteration)
            sp.wait_ge(s_sum0, NB)
            sp.dma_start(out[0:HID, :], sums0[HID:P, :]).then_inc(s_out, 16)
            sp.wait_ge(s_sum1, NB)
            sp.dma_start(out[HID:HID + P, :], sums1[:, :]).then_inc(s_out, 16)
            sp.wait_ge(s_out, 32)

        @block.gpsimd
        def _(pool):
            nc.gpsimd.memset(picks, 0.0).then_inc(s_pick0, 1)
            pool.wait_ge(s_pick0, 1)
            for part in range(2):
                v = picks[part * F:(part + 1) * F, :].rearrange("p (t g h) -> p t g h", t=8, g=KK)
                nc.gpsimd.affine_select(out=v, in_=v, compare_op=ALU.not_equal, fill=1.0, base=0,
                                        pattern=[[-KK, 8], [-1, KK], [0, F]],
                                        channel_multiplier=1).then_inc(s_pick1, 1)

            last = [s_pick1, 2]

            def settle():
                pool.wait_ge(*last)

            def done(instruction, s, value):
                instruction.then_inc(s, 1)
                last[:] = [s, value]

            pool.wait_ge(s_rot16_zero, 1)
            settle()

            def square(n, past):
                pool.wait_ge(s_x4_in[n % 2], landed(KK, n, past))
                pool.wait_ge(s_rot_in[n % 2], landed(KK, n, past))
                done(nc.gpsimd.tensor_tensor(rot[:, n % 2], x4[:, n % 2, :].unsqueeze(1).broadcast_to([P, 4, C]),
                                             rot[:, n % 2], ALU.mult), s_square, n + 1 + past)

            def rest(n, past):
                pool.wait_ge(s_rot16_in[n % 2], landed(2, n, past))
                if n >= 1:
                    pool.wait_ge(s_rest_low, n + past)
                done(nc.gpsimd.tensor_tensor(zr[:, :], x4[:, n % 2, :], rot16[:, n % 2, :], ALU.mult),
                     s_rest, n + 1 + past)

            def square_low(n, past):
                pool.wait_ge(s_square_high, n + 1 + past)
                done(nc.gpsimd.tensor_tensor(sql[:, n % SQ_RING], rot[:, n % 2], sqh[:, n % SQ_RING], ALU.subtract),
                     s_square_low, n + 1 + past)

            def rest_low(n, past):
                pool.wait_ge(s_rest_high, n + 1 + past)
                settle()
                done(nc.gpsimd.tensor_tensor(zrs[F:2 * F, :], zr[F:2 * F, :], zrs[F:2 * F, :],
                                             ALU.subtract), s_rest_low, n + 1 + past)
                settle()

            def x_low(n, past):
                pool.wait_ge(s_x_high, n + 1 + past)
                settle()
                xsn = xs[F:2 * F, n % XS_RING, :]
                done(nc.gpsimd.tensor_tensor(xsn, x4[F:2 * F, n % 2, :], xsn, ALU.subtract), s_x_low, n + 1 + past)
                settle()

            def low_a(b, past):
                for v in A_SPLIT:
                    pool.wait_ge(s_a_high, a_splits_done(b, v, past))
                    r = (a_splits_done(b, v, 0) - 1) % A_RING
                    done(nc.gpsimd.tensor_tensor(al[:, r], za[:, unit(b, v) % Z_RING], ah[:, r], ALU.subtract),
                         s_a_low, a_splits_done(b, v, past))

            steps = {"square": square, "rest": rest, "square_low": square_low, "rest_low": rest_low, "x_low": x_low}

            def iteration(b, past):
                for name in POOL_ORDER:
                    if name == "low_a":
                        if b >= 0:
                            low_a(b, past)
                    elif b + AHEAD <= LAST:
                        steps[name](b + AHEAD, past)

            blocks(pool, iteration)

        @block.scalar
        def _(act):
            act.dma_start(w0a, w0_near[0:512, :].rearrange("(j p) o -> p j o", p=P)).then_inc(s_w0_in, 16)
            act.dma_start(w0b[:, 1:4, :], w0_far[128:512, :].rearrange("(j p) o -> p j o", p=P)).then_inc(s_w0_in, 16)
            act.dma_start(w0b[F:P, 0, :], w0_far[F:P, :]).then_inc(s_w0_in, 16)
            for g in range(2):
                act.dma_start(ra[g * F:(g + 1) * F, :], w0_near[512:544, :]).then_inc(s_wr_in, 16)
                act.dma_start(rb[g * F:(g + 1) * F, :], w0_far[512:544, :]).then_inc(s_wr_in, 16)
            act.dma_start(bias0[:, :], b0).then_inc(s_b_in, 16)
            act.dma_start(bias1[:, :], b1).then_inc(s_b_in, 16)
            act.dma_start(za[:, 0:2].rearrange("p r k c -> p (r k c)"), w1_tiles).then_inc(s_w1_in, 16)

            act.wait_ge(s_w0_sum, 1)
            nc.scalar.activation(w0h[:, :, :], w0s, ACT.Copy).then_inc(s_w0_high, 1)
            act.wait_ge(s_pick1, 2)
            nc.scalar.activation(pick[:, :, :].rearrange("p t o -> p (t o)"), picks, ACT.Copy).then_inc(s_pick, 1)
            act.wait_ge(s_wr_sum, 1)
            act.wait_ge(s_zeros, 2)
            nc.scalar.activation(wr[0:2 * F, :], rs[0:2 * F, :], ACT.Copy).then_inc(s_wr_high, 1)
            act.wait_ge(s_b_in, 32)

            def square_high(n, past):
                act.wait_ge(s_square, n + 1 + past)
                if n >= SQ_RING:
                    act.wait_ge(s_square_used, n + 1 - SQ_RING + past)
                nc.scalar.activation(sqh[:, n % SQ_RING], rot[:, n % 2], ACT.Copy).then_inc(s_square_high, 1)

            def rest_high(n, past):
                act.wait_ge(s_rest, n + 1 + past)
                if n >= 1:
                    act.wait_ge(s_rest_used, n + past)
                nc.scalar.activation(zrs[:, :], zr[:, :], ACT.Copy).then_inc(s_rest_high, 1)

            def x_high(n, past):
                act.wait_ge(s_x4_in[n % 2], landed(KK, n, past))
                if n >= XS_RING:
                    act.wait_ge(s_xb, units_done(n - XS_RING, UNITS - 1, past))
                nc.scalar.activation(xs[:, n % XS_RING, :], x4[:, n % 2, :], ACT.Copy).then_inc(s_x_high, 1)

            def relu0(n, past):
                act.wait_ge(s_rest_used, n + 1 + past)
                if n >= 1:
                    act.wait_ge(s_hid_in[(n - 1) % 2], landed(2 * KK, n - 1, past))
                    act.wait_ge(s_sum0, n + past)
                nc.scalar.activation(y0r[:, :], y0[:, :], ACT.Relu, bias=bias0[:, :]).then_inc(s_relu0, 1)

            def relu1(b, past):
                act.wait_ge(s_unit_used, units_done(b, UNITS - 1, past))
                if b >= 1:
                    act.wait_ge(s_sum1, b + past)
                nc.scalar.activation(y1r[:, :], y1[:, :], ACT.Relu, bias=bias1[:, :]).then_inc(s_relu1, 1)

            def unit_high(b, v, past):
                if v in A_SPLIT:
                    act.wait_ge(s_a, units_done(b, v, past))
                    k = a_splits_done(b, v, 0) - 1
                    if k >= A_RING:
                        old = b - A_RING // len(A_SPLIT)
                        act.wait_ge(s_unit_used, units_done(old, v, past))
                    nc.scalar.activation(ah[:, k % A_RING], za[:, unit(b, v) % Z_RING],
                                         ACT.Copy).then_inc(s_a_high, 1)
                act.wait_ge(s_b, units_done(b, v, past))
                if unit(b, v) >= B_RING:
                    act.wait_ge(s_unit_used, units_done(b, v, past) - B_RING)
                nc.scalar.activation(bh[:, unit(b, v) % B_RING], xb_of(b, v), ACT.Copy).then_inc(s_b_high, 1)

            def iteration(b, past):
                n = b + AHEAD
                for v in range(UNITS):
                    if b >= 0:
                        unit_high(b, v, past)
                    for name, step in (("square_high", square_high), ("rest_high", rest_high), ("x_high", x_high)):
                        if ACT_STEPS[name] == v and n <= LAST:
                            step(n, past)
                    if ACT_STEPS["relu1"] == v and b >= 1:
                        relu1(b - 1, past)
                    if ACT_STEPS["relu0"] == v and 0 <= n - 1 <= LAST:
                        relu0(n - 1, past)
                if b == -AHEAD:
                    act.wait_ge(s_w1_in, 16)
                    for v in range(UNITS):
                        nc.scalar.activation(w1h[:, v], w1raw[:, v, 1], ACT.Copy).then_inc(s_w1_high, 1)
                    for k, v in enumerate(A_SPLIT):
                        nc.scalar.activation(w1h[:, UNITS + k], w1raw[:, v, 0], ACT.Copy).then_inc(s_w1_high, 1)

            blocks(act, iteration)
            relu1(LAST, 0)

        @block.vector
        def _(dve):
            nc.vector.memset(rot16[HID:P, :, :], 0.0).then_inc(s_rot16_zero, 1)
            nc.vector.memset(w0b[0:F, 0, :], 0.0).then_inc(s_zeros, 1)
            nc.vector.memset(wr[:, :].bitcast(F32), 0.0).then_inc(s_zeros, 1)
            dve.wait_ge(s_zeros, 1)
            dve.wait_ge(s_w0_in, 48)
            nc.vector.tensor_tensor(w0s, w0a, w0b, ALU.add).then_inc(s_w0_sum, 1)
            dve.wait_ge(s_wr_in, 64)
            nc.vector.tensor_tensor(rs[0:2 * F, :], ra[0:2 * F, :], rb[0:2 * F, :], ALU.add).then_inc(s_wr_sum, 1)
            dve.wait_ge(s_w0_high, 1)
            nc.vector.tensor_tensor(w0l[:, :, :], w0s, w0h[:, :, :], ALU.subtract).then_inc(s_w0_low, 1)
            dve.wait_ge(s_wr_high, 1)
            nc.vector.tensor_tensor(wr_low[0:2 * F, :], rs[0:2 * F, :], wr[0:2 * F, :],
                                    ALU.subtract).then_inc(s_wr_low, 1)
            dve.wait_ge(s_w1_in, 16)
            for k, v in enumerate(A_NATIVE):
                nc.vector.tensor_copy(w1n[:, k], w1raw[:, v, 0]).then_inc(s_w1_whole, 1)
            for k in range(N_SPLIT):
                dve.wait_ge(s_w1_high, k + 1)
                w = w1raw[:, k, 1] if k < UNITS else w1raw[:, A_SPLIT[k - UNITS], 0]
                nc.vector.tensor_tensor(w1l[:, k], w, w1h[:, k], ALU.subtract).then_inc(s_w1_low, 1)
            dve.wait_ge(s_w1_low, N_SPLIT)
            dve.wait_ge(s_w1_whole, len(A_NATIVE))
            dve.wait_ge(s_w0_low, 1)
            dve.wait_ge(s_wr_low, 1)

            def form_a(b, v, past):
                u = unit(b, v)
                if v == 0:
                    dve.wait_ge(s_hid_in[b % 2], landed(2 * KK, b, past))
                if u >= Z_RING:
                    old_b, old_v = divmod(u - Z_RING, UNITS)
                    if old_v in A_SPLIT:
                        dve.wait_ge(s_a_low, a_splits_done(old_b, old_v, past))
                    else:
                        dve.wait_ge(s_unit_used, units_done(old_b, old_v, past))
                dve.wait_ge(s_xb, units_done(b, v, past))
                hidden = hid4[:, b % HID_RING, 0, :].unsqueeze(1).broadcast_to([P, 2, C])
                nc.vector.tensor_tensor(za[:, u % Z_RING], xb_of(b, v), hidden, ALU.mult).then_inc(s_a, 1)

            def form_b(b, v, past):
                dve.wait_ge(s_a, units_done(b, v, past))
                hidden = hid4[:, b % HID_RING, 1, :].unsqueeze(1).broadcast_to([P, 2, C])
                nc.vector.tensor_tensor(xb_of(b, v), xb_of(b, v), hidden, ALU.mult).then_inc(s_b, 1)

            def low_b(b, v, past):
                dve.wait_ge(s_b_high, units_done(b, v, past))
                r = unit(b, v) % B_RING
                nc.vector.tensor_tensor(bl[:, r], xb_of(b, v), bh[:, r], ALU.subtract).then_inc(s_b_low, 1)

            def sum0(n, past):
                dve.wait_ge(s_relu0, n + 1 + past)
                nc.vector.tensor_reduce(sums0[HID:P, bass.ds(n * SB + SB * past, SB)],
                                        y0r[HID:P, :].rearrange("p (s d) -> p s d", d=D), AX_X,
                                        ALU.add).then_inc(s_sum0, 1)

            def sum1(b, past):
                dve.wait_ge(s_relu1, b + 1 + past)
                nc.vector.tensor_reduce(sums1[:, bass.ds(b * SB + SB * past, SB)],
                                        y1r[:, :].rearrange("p (s d) -> p s d", d=D), AX_X,
                                        ALU.add).then_inc(s_sum1, 1)

            def iteration(b, past):
                n = b + AHEAD
                for v in range(UNITS):
                    if b >= 0:
                        form_a(b, v, past)
                        if (b, v) != (0, 0):
                            low_b(*((b, v - 1) if v else (b - 1, UNITS - 1)), past)
                        form_b(b, v, past)
                    if DVE_STEPS["sum1"] == v and b >= 1:
                        sum1(b - 1, past)
                    if DVE_STEPS["sum0"] == v and 0 <= n - 1 <= LAST:
                        sum0(n - 1, past)

            blocks(dve, iteration)
            low_b(LAST, UNITS - 1, 0)
            sum1(LAST, 0)

        @block.tensor
        def _(pe):
            pe.wait_ge(s_w0_high, 1)
            pe.wait_ge(s_w0_low, 1)
            pe.wait_ge(s_pick, 1)

            def layer0(n, past):
                if n >= 1:
                    pe.wait_ge(s_relu0, n + past)
                pe.wait_ge(s_square_high, n + 1 + past)
                for j in range(4):
                    for w in (w0h, w0l):
                        nc.tensor.matmul(y0[:, :], w[:, j, :], sqh[:, n % SQ_RING, j, :], start=j == 0 and w is w0h, stop=False)
                pe.wait_ge(s_square_low, n + 1 + past)
                for j in range(4):
                    last = nc.tensor.matmul(y0[:, :], w0h[:, j, :], sql[:, n % SQ_RING, j, :], start=False, stop=False)
                last.then_inc(s_square_used, 1)
                if n == 0:
                    pe.wait_ge(s_wr_put, 32)
                pe.wait_ge(s_rest_low, n + 1 + past)
                nc.tensor.matmul(y0[:, :], wr[:, :], zrs[:, :], start=False, stop=True).then_inc(s_rest_used, 1)

            def broadcast(b, v, past):
                if v == 0:
                    pe.wait_ge(s_x_low, b + 1 + past)
                if unit(b, v) >= XB_RING:
                    pe.wait_ge(s_b_low, units_done(b, v, past) - XB_RING)
                for k in range(2):
                    last = nc.tensor.matmul(xb[:, place(b, v), k, :], pick[:, 2 * v + k, :],
                                            xs[:, b % XS_RING, :], start=True, stop=True)
                last.then_inc(s_xb, 1)

            def split_terms(s_high, s_low, value, k_w, high, low, start, stop):
                pe.wait_ge(s_high, value)
                for k in range(2):
                    for w in (w1h, w1l):
                        nc.tensor.matmul(y1[:, :], w[:, k_w, k, :], high[:, k, :],
                                         start=start and k == 0 and w is w1h, stop=False)
                pe.wait_ge(s_low, value)
                for k in range(2):
                    last = nc.tensor.matmul(y1[:, :], w1h[:, k_w, k, :], low[:, k, :],
                                            start=False, stop=stop and k == 1)
                return last

            def contract_a(b, v, past):
                if v == 0 and b >= 1:
                    pe.wait_ge(s_relu1, b + past)
                if (b, v) == (0, 0):
                    pe.wait_ge(s_w1_low, N_SPLIT)
                    pe.wait_ge(s_w1_whole, len(A_NATIVE))
                if v in A_SPLIT:
                    r = (a_splits_done(b, v, 0) - 1) % A_RING
                    split_terms(s_a_high, s_a_low, a_splits_done(b, v, past), UNITS + A_SPLIT.index(v),
                                ah[:, r], al[:, r], v == 0, False)
                else:
                    pe.wait_ge(s_a, units_done(b, v, past))
                    for k in range(2):
                        nc.tensor.matmul(y1[:, :], w1n[:, A_NATIVE.index(v), k, :], za[:, unit(b, v) % Z_RING, k, :],
                                         start=v == 0 and k == 0, stop=False)

            def contract_b(b, v, past):
                r = unit(b, v) % B_RING
                split_terms(s_b_high, s_b_low, units_done(b, v, past), v, bh[:, r], bl[:, r],
                            False, v == UNITS - 1).then_inc(s_unit_used, 1)

            def iteration(b, past):
                n = b + AHEAD
                for v in range(UNITS):
                    for half, contract in enumerate((contract_a, contract_b)):
                        if half == 0 and v == L0_AFTER and n <= LAST:
                            layer0(n, past)
                        for k, at in enumerate(XB_AT):
                            ahead_b, ahead_v = divmod(unit(b, k) + XB_LEAD, UNITS)
                            if at == (v, half) and 0 <= ahead_b <= LAST:
                                broadcast(ahead_b, ahead_v, past)
                        if b >= 0:
                            contract(b, v, past)

            blocks(pe, iteration)


def kernel(r_cin_inputs, L0_rec_w0, L0_rec_b0, L0_rec_w1, L0_rec_b1):
    import numpy as np
    import concourse.bacc as bacc
    from concourse.bass_utils import run_bass_kernel_spmd

    x = np.asarray(r_cin_inputs)
    B, F_, D_ = x.shape
    x = x.transpose(1, 0, 2).reshape(F_, B * D_)
    x_rows = np.ascontiguousarray(np.concatenate([x, x[:16]], axis=0))
    w0 = np.asarray(L0_rec_w0).T.reshape(F_, F_, -1)
    i = np.arange(F_)
    near = np.stack([w0[i, (i + k) % F_] for k in range(17)]).reshape(17 * F_, -1)
    far = np.stack([w0[(i + k) % F_, i] for k in range(17)]).reshape(17 * F_, -1)
    w1 = np.asarray(L0_rec_w1).T.reshape(2, 32, 4, 2, 4, -1).transpose(4, 1, 2, 0, 3, 5).reshape(128, -1)
    arrays = {
        "x_rows": x_rows,
        "w0_near": np.ascontiguousarray(near),
        "w0_far": np.ascontiguousarray(far),
        "w1_tiles": np.ascontiguousarray(w1),
        "b0": np.ascontiguousarray(np.asarray(L0_rec_b0).reshape(-1, 1)),
        "b1": np.ascontiguousarray(np.asarray(L0_rec_b1).reshape(-1, 1)),
    }
    nc = bacc.Bacc("TRN2", target_bir_lowering=False, num_devices=1)
    args = [nc.dram_tensor(name, a.shape, mybir.dt.from_np(a.dtype), kind="ExternalInput").ap()
            for name, a in arrays.items()]
    args.append(nc.dram_tensor("out", (192, B), F32, kind="ExternalOutput").ap())
    cin_kernel(nc, *args)
    r = run_bass_kernel_spmd(nc, [arrays], core_ids=[0])
    return np.ascontiguousarray(r.results[0]["out"].T)
```

```python
from contextlib import ExitStack

import concourse.bass as bass
from concourse import mybir

F32 = mybir.dt.float32
F32R = mybir.dt.float32r
ALU = mybir.AluOpType
ACT = mybir.ActivationFunctionType
AX_X = mybir.AxisListType.X

P = 128
F = 32
HID = 64
D = 64
C = 512
KK = P // F
G = 8
H = P // G
UNITS = F // G
QUARTERS = HID // H
AHEAD = 2
A_TILES_SPLIT = {2: 2, 3: 1}
A_SPLIT = tuple(A_TILES_SPLIT)
A_NATIVE = tuple(v for v in range(UNITS) if A_TILES_SPLIT.get(v, 0) < 2)
NATIVE0 = 3
SQUARES_DVE = 2
WARM_UP = 6
XB_LEAD = 3
HEAD = 6
BODY = 6
PE_ORDER = (('X', 0), ('X', 1), ('A', 0), ('A', 1), ('B', 0), ('X', 2), ('B', 1), ('layer0', 0),
            ('A', 2), ('B', 2), ('X', 3), ('A', 3), ('B', 3))
PE_ORDER_FIRST = (('layer0 of 1', 0), ('A', 0), ('X', 0), ('B', 0), ('A', 1), ('X', 1), ('B', 1),
                  ('layer0', 0), ('A', 2), ('X', 2), ('B', 2), ('A', 3), ('X', 3), ('B', 3))
DVE_ORDER = (('A', 0), ('L', -1), ('B', 0), ('A', 1), ('L', 0), ('B', 1), ('A', 2), ('L', 1),
             ('B', 2), ('sum1', 0), ('A', 3), ('L', 2), ('B', 3))
ACT_ORDER = (('B', 0), ('relu0', 0), ('square_high', 0), ('B', 1), ('relu1', 0), ('sum0', 0),
             ('sum0', 1), ('xz_high', 0), ('sum0', 2), ('A', 2), ('B', 2), ('sum0', 3),
             ('sum0', 4), ('sum0', 5), ('sum0', 6), ('A', 3), ('B', 3), ('sum0', 7))
POOL_ORDER = (('square', 0), ('low_a', -1), ('xz', 0), ('square_low', 0), ('xz_low', 0),
              ('low_a', 2))
XB_RING, ZB_RING = 4, 1
Z_RING, B_RING, A_RING, SQ_RING, HID_RING, XZ_RING = 6, 4, 2, 2, 3, 3


def cin_kernel(nc: bass.Bass, x_rows, w0_near, w0_far, w1_tiles, b0, b1, out):
    N = x_rows.shape[1]
    NB = N // C
    SB = C // D
    LAST = NB - 1

    def unit(b, v):
        return UNITS * b + v

    def units_done(b, v, past):
        return unit(b, v) + 1 + UNITS * past

    def a_splits_done(b, v, past):
        return len(A_SPLIT) * b + sum(s <= v for s in A_SPLIT) + len(A_SPLIT) * past

    assert BODY * len(A_SPLIT) % A_RING == BODY % SQ_RING == BODY % HID_RING == BODY % XZ_RING == BODY % 2 == 0
    assert all(BODY * UNITS % ring == 0 for ring in (Z_RING, B_RING, XB_RING, ZB_RING))

    ctx = ExitStack()
    with ctx:
        def sb(name, shape, dt=F32):
            return ctx.enter_context(nc.sbuf_tensor(name, shape, dt))

        def sem(name):
            return ctx.enter_context(nc.semaphore(name))

        N_SPLIT = UNITS + len(A_SPLIT)
        w0s, rs = sb("w0s", [P, 4, P]), sb("rs", [P, P])
        w0h, w0l = sb("w0h", [P, 4, P], F32R), sb("w0l", [P, 4, P], F32R)
        w1h, w1l = sb("w1h", [P, N_SPLIT, 2, P], F32R), sb("w1l", [P, N_SPLIT, 2, P], F32R)
        w1n = sb("w1n", [P, len(A_NATIVE), 2, P])
        wr = sb("wr", [P, P], F32R)
        wr_high, wr_low = sb("wr_high", [P, P], F32R), sb("wr_low", [P, P], F32R)
        pick = sb("pick", [P, UNITS, P], F32R)
        bias0, bias1 = sb("bias0", [P, 1]), sb("bias1", [P, 1])
        x4 = sb("x4", [P, 2, C])
        rot = sb("rot", [P, 2, 4, C])
        rot16 = sb("rot16", [P, 2, C])
        xz, xzs = sb("xz", [P, C]), sb("xzs", [P, XZ_RING, C], F32R)
        sqh, sql = sb("sqh", [P, SQ_RING, 4, C], F32R), sb("sql", [P, SQ_RING, 4, C], F32R)
        za = sb("za", [P, Z_RING, 2, C])
        bh, bl = sb("bh", [P, B_RING, 2, C], F32R), sb("bl", [P, B_RING, 2, C], F32R)
        ah, al = sb("ah", [P, A_RING, 2, C], F32R), sb("al", [P, A_RING, 2, C], F32R)
        y0r, y1r = sb("y0r", [P, C]), sb("y1r", [P, C])
        hid8 = sb("hid8", [P, HID_RING, QUARTERS, C])
        sums0, sums1 = sb("sums0", [P, N // D]), sb("sums1", [P, N // D])

        y = ctx.enter_context(nc.psum_tensor("y", [P, 2, C], F32))
        xb = ctx.enter_context(nc.psum_tensor("xb", [P, XB_RING, C], F32))
        zb = ctx.enter_context(nc.psum_tensor("zb", [P, ZB_RING, 2, C], F32))

        w1raw = za[:, 0:2].rearrange("p r k (c o) -> p (r k c) o", o=P).rearrange(
            "p (v h k) o -> p v h k o", h=2, k=2)
        w0a = za[:, 2, 0, :].rearrange("p (j o) -> p j o", j=4)
        w0b = za[:, 2, 1, :].rearrange("p (j o) -> p j o", j=4)
        ra, rb = za[:, 3, 1, 0:P], za[:, 3, 1, P:2 * P]
        picks = hid8[:, HID_RING - 1, 0]

        s_w0_in, s_wr_in, s_w1_in, s_b_in = sem("s_w0_in"), sem("s_wr_in"), sem("s_w1_in"), sem("s_b_in")
        s_zeros, s_ones, s_warm_zero = sem("s_zeros"), sem("s_ones"), sem("s_warm_zero")
        s_w0_sum, s_w0_high, s_w0_low = sem("s_w0_sum"), sem("s_w0_high"), sem("s_w0_low")
        s_wr_sum, s_wr_high, s_wr_low, s_wr_put = sem("s_wr_sum"), sem("s_wr_high"), sem("s_wr_low"), sem("s_wr_put")
        s_w1_high, s_w1_low, s_w1_whole = sem("s_w1_high"), sem("s_w1_low"), sem("s_w1_whole")
        s_pick0, s_pick1, s_pick = sem("s_pick0"), sem("s_pick1"), sem("s_pick")
        s_x4_in = [sem("s_x4_in0"), sem("s_x4_in1")]
        s_rot_in = [sem("s_rot_in0"), sem("s_rot_in1")]
        s_first_rot_in = sem("s_first_rot_in")
        s_rot16_in = [sem("s_rot16_in0"), sem("s_rot16_in1")]
        s_hid_a_in = [sem("s_hid_a_in0"), sem("s_hid_a_in1")]
        s_hid_b_in = [sem("s_hid_b_in0"), sem("s_hid_b_in1")]
        s_first_squares = sem("s_first_squares")
        s_square, s_square_high, s_square_low = sem("s_square"), sem("s_square_high"), sem("s_square_low")
        s_square_used, s_rest_used = sem("s_square_used"), sem("s_rest_used")
        s_xz, s_xz_high, s_xz_low = sem("s_xz"), sem("s_xz_high"), sem("s_xz_low")
        s_xb, s_unit_used = sem("s_xb"), sem("s_unit_used")
        s_a, s_b, s_b_high, s_b_low = sem("s_a"), sem("s_b"), sem("s_b_high"), sem("s_b_low")
        s_a_high, s_a_low = sem("s_a_high"), sem("s_a_low")
        s_relu0, s_relu1, s_sum0, s_sum1 = sem("s_relu0"), sem("s_relu1"), sem("s_sum0"), sem("s_sum1")
        s_out = sem("s_out")

        def blocks(eng, iteration):
            first = HEAD - AHEAD
            trips = (NB - AHEAD - 2 - first) // BODY
            for b in range(-AHEAD, first):
                iteration(b, 0)
            with eng.Fori(0, trips) as trip:
                for b in range(first, first + BODY):
                    iteration(b, trip * BODY)
            for b in range(first + BODY * trips, NB):
                iteration(b, 0)

        def xb_of(b, v):
            return xb[:, unit(b, v) % XB_RING]

        def y1_of(b):
            return y[:, b % 2, :]

        def y0_of(n):
            return y[:, 1 if n == 1 else (n - 1) % 2, :]

        def zb_of(b, v):
            return zb[:, unit(b, v) % ZB_RING]

        def landed(dmas, n, past):
            return 16 * dmas * (n // 2 + 1) + 8 * dmas * past

        def rot_landed(n, past):
            return landed(4, n, past) - 32 * (n % 2 == 0)

        def squares_done(n, past):
            return n + 1 - SQUARES_DVE + past

        def splits0_done(n, past):
            return n + 1 - NATIVE0 + past

        block = ctx.enter_context(nc.Block())

        @block.sync
        def _(sp):
            def load(n, past):
                cols = bass.ds(n * C + C * past, C)

                def load_rot(j, s_in=s_rot_in[n % 2]):
                    rows = bass.AP(x_rows.tensor, x_rows.offset + KK * j * N, [[N, KK], [N, F], [1, N]])
                    sp.dma_start(rot[:, n % 2, j, :], rows[:, :, cols]).then_inc(s_in, 16)

                def load_x4():
                    rows = bass.AP(x_rows.tensor, x_rows.offset, [[0, KK], [N, F], [1, N]])
                    sp.dma_start(x4[:, n % 2, :], rows[:, :, cols]).then_inc(s_x4_in[n % 2], 16)

                def load_rot16():
                    for row in (F, 3 * F):
                        sp.dma_start(rot16[row:row + F, n % 2, :],
                                     x_rows[16:16 + F, cols]).then_inc(s_rot16_in[n % 2], 16)

                if n < 2:
                    load_x4()
                    for j in range(2):
                        load_rot(j, s_first_rot_in if n == 0 else s_rot_in[n])
                    if n == 0:
                        sp.wait_ge(s_ones, 1)
                    load_rot16()
                    load_rot(2)
                    load_rot(3)
                    return
                sp.wait_ge(s_square_used, n - 1 + past)
                for j in range(4):
                    load_rot(j)
                sp.wait_ge(s_xz, n - 1 + past)
                load_x4()
                load_rot16()

            def copy_hidden(n, past):
                sp.wait_ge(s_relu0, n + 1 + past)
                for q in range(QUARTERS):
                    s_in = (s_hid_a_in, s_hid_b_in)[q // 2][n % 2]
                    copies = y0r[q * H:(q + 1) * H, :].unsqueeze(1).broadcast_to([H, G, C])
                    sp.dma_start(hid8[:, n % HID_RING, q, :], copies).then_inc(s_in, 16)

            load(0, 0)
            for raw, w in ((ra, w0_near), (rb, w0_far)):
                rows = bass.AP(w.tensor, w.offset + 512 * P, [[0, KK], [P, F], [1, P]])
                sp.dma_start(raw, rows).then_inc(s_wr_in, 16)
            sp.dma_start(bias0[:, :], b0).then_inc(s_b_in, 16)
            sp.dma_start(bias1[:, :], b1).then_inc(s_b_in, 16)
            sp.dma_start(za[:, 0:2].rearrange("p r k c -> p (r k c)"), w1_tiles).then_inc(s_w1_in, 16)
            load(1, 0)

            def put_wr():
                sp.wait_ge(s_zeros, 2)
                sp.wait_ge(s_wr_high, 1)
                sp.wait_ge(s_wr_low, 1)
                for row, w in ((F, wr_high), (F + 16, wr_low), (3 * F, wr_high), (3 * F + 16, wr_low)):
                    rows = slice(row, row + 16)
                    sp.dma_start(wr[rows, :].bitcast(F32), w[rows, :].bitcast(F32)).then_inc(s_wr_put, 16)

            def iteration(b, past):
                n = b + AHEAD
                if n == 0:
                    copy_hidden(0, 0)
                    load(2, 0)
                    return
                if n <= LAST:
                    copy_hidden(n, past)
                if n + 2 <= LAST:
                    load(n + 2, past)
                if n == 1:
                    put_wr()

            blocks(sp, iteration)
            sp.wait_ge(s_sum0, SB * NB)
            sp.dma_start(out[0:HID, :], sums0[HID:P, :]).then_inc(s_out, 16)
            sp.wait_ge(s_sum1, NB)
            sp.dma_start(out[HID:HID + P, :], sums1[:, :]).then_inc(s_out, 16)
            sp.wait_ge(s_out, 32)

        @block.gpsimd
        def _(pool):
            nc.gpsimd.memset(picks, 0.0).then_inc(s_pick0, 1)
            pool.wait_ge(s_pick0, 1)
            for part in range(2):
                v = picks[2 * F * part:2 * F * part + F, :].rearrange("p (t h g) -> p t h g", t=UNITS, g=G)
                nc.gpsimd.affine_select(out=v, in_=v, compare_op=ALU.not_equal, fill=1.0, base=0,
                                        pattern=[[-G, UNITS], [0, H], [-1, G]],
                                        channel_multiplier=1).then_inc(s_pick1, 1)

            last = [s_pick1, 2]

            def settle():
                pool.wait_ge(*last)

            def done(instruction, s, value):
                instruction.then_inc(s, 1)
                last[:] = [s, value]

            pool.wait_ge(s_ones, 1)
            settle()

            def square(n, past):
                pool.wait_ge(s_x4_in[n % 2], landed(1, n, past))
                pool.wait_ge(s_rot_in[n % 2], rot_landed(n, past))
                done(nc.gpsimd.tensor_tensor(rot[:, n % 2], x4[:, n % 2, :].unsqueeze(1).broadcast_to([P, 4, C]),
                                             rot[:, n % 2], ALU.mult), s_square, squares_done(n, past))

            def xz_products(n, past):
                if n < SQUARES_DVE:
                    pool.wait_ge(s_x4_in[n], 16)
                pool.wait_ge(s_rot16_in[n % 2], landed(2, n, past))
                if n >= 1:
                    pool.wait_ge(s_xz_low, n + past)
                if 1 <= n <= NATIVE0:
                    pool.wait_ge(s_rest_used, n)
                done(nc.gpsimd.tensor_tensor(xz[:, :], x4[:, n % 2, :], rot16[:, n % 2, :], ALU.mult),
                     s_xz, n + 1 + past)

            def square_low(n, past):
                pool.wait_ge(s_square_high, splits0_done(n, past))
                done(nc.gpsimd.tensor_tensor(sql[:, n % SQ_RING], rot[:, n % 2], sqh[:, n % SQ_RING], ALU.subtract),
                     s_square_low, splits0_done(n, past))

            def xz_low(n, past):
                pool.wait_ge(s_xz_high, n + 1 + past)
                settle()
                part = xzs[2 * F:P, n % XZ_RING, :]
                done(nc.gpsimd.tensor_tensor(part, xz[2 * F:P, :], part, ALU.subtract), s_xz_low, n + 1 + past)
                settle()

            def low_a(b, v, past):
                k, tiles = a_splits_done(b, v, 0) - 1, A_TILES_SPLIT[v]
                pool.wait_ge(s_a_high, a_splits_done(b, v, past))
                done(nc.gpsimd.tensor_tensor(al[:, k % A_RING, 0:tiles], za[:, unit(b, v) % Z_RING, 0:tiles],
                                             ah[:, k % A_RING, 0:tiles], ALU.subtract),
                     s_a_low, a_splits_done(b, v, past))

            steps = {"square": square, "xz": xz_products, "square_low": square_low, "xz_low": xz_low}

            def iteration(b, past):
                n = b + AHEAD
                if n < NATIVE0:
                    if n >= SQUARES_DVE:
                        square(n, 0)
                    xz_products(n, 0)
                    xz_low(n, 0)
                for name, v in POOL_ORDER:
                    if name == "low_a":
                        if v >= 0 and b >= 0:
                            low_a(b, v, past)
                        elif v < 0 and b >= 1:
                            low_a(b - 1, UNITS + v, past)
                    elif NATIVE0 <= n <= LAST:
                        steps[name](n, past)

            blocks(pool, iteration)
            for name, v in POOL_ORDER:
                if name == "low_a" and v < 0:
                    low_a(LAST, UNITS + v, 0)

        @block.scalar
        def _(act):
            act.dma_start(w0a, w0_near[0:512, :].rearrange("(j p) o -> p j o", p=P)).then_inc(s_w0_in, 16)
            act.dma_start(w0b[:, 1:4, :], w0_far[128:512, :].rearrange("(j p) o -> p j o", p=P)).then_inc(s_w0_in, 16)
            act.dma_start(w0b[F:P, 0, :], w0_far[F:P, :]).then_inc(s_w0_in, 16)
            act.wait_ge(s_pick1, 2)
            nc.scalar.activation(pick[:, :, :].rearrange("p t o -> p (t o)"), picks, ACT.Copy).then_inc(s_pick, 1)

            def square_high(n, past):
                act.wait_ge(s_square, squares_done(n, past))
                if n >= NATIVE0 + SQ_RING:
                    act.wait_ge(s_square_used, n + 1 - SQ_RING + past)
                nc.scalar.activation(sqh[:, n % SQ_RING], rot[:, n % 2], ACT.Copy).then_inc(s_square_high, 1)

            def xz_high(n, past):
                act.wait_ge(s_xz, n + 1 + past)
                if n >= XZ_RING:
                    act.wait_ge(s_xb, units_done(n - XZ_RING, UNITS - 1, past))
                nc.scalar.activation(xzs[:, n % XZ_RING, :], xz[:, :], ACT.Copy).then_inc(s_xz_high, 1)

            def relu0(n, past):
                if n == 0:
                    act.wait_ge(s_b_in, 32)
                act.wait_ge(s_rest_used, n + 1 + past)
                if n >= 1:
                    act.wait_ge(s_hid_a_in[(n - 1) % 2], landed(2, n - 1, past))
                    act.wait_ge(s_hid_b_in[(n - 1) % 2], landed(2, n - 1, past))
                    act.wait_ge(s_sum0, SB * n + SB * past)
                nc.scalar.activation(y0r[:, :], y0_of(n), ACT.Relu, bias=bias0[:, :]).then_inc(s_relu0, 1)

            def sum0(n, i, past):
                act.wait_ge(s_relu0, n + 1 + past)
                rows = y0r[HID:P, i * D:(i + 1) * D]
                nc.scalar.activation(rows, rows, ACT.Copy, accum_out=sums0[HID:P, bass.ds(n * SB + i + SB * past, 1)]
                                     ).then_inc(s_sum0, 1)

            def relu1(b, past):
                act.wait_ge(s_unit_used, units_done(b, UNITS - 1, past))
                if b >= 1:
                    act.wait_ge(s_sum1, b + past)
                nc.scalar.activation(y1r[:, :], y1_of(b), ACT.Relu, bias=bias1[:, :]).then_inc(s_relu1, 1)

            def high_a(b, v, past):
                act.wait_ge(s_a, units_done(b, v, past))
                k = a_splits_done(b, v, 0) - 1
                if k >= A_RING:
                    old = b - A_RING // len(A_SPLIT)
                    act.wait_ge(s_unit_used, units_done(old, v, past))
                tiles = A_TILES_SPLIT[v]
                nc.scalar.activation(ah[:, k % A_RING, 0:tiles], za[:, unit(b, v) % Z_RING, 0:tiles],
                                     ACT.Copy).then_inc(s_a_high, 1)

            def high_b(b, v, past):
                act.wait_ge(s_b, units_done(b, v, past))
                if unit(b, v) >= B_RING:
                    act.wait_ge(s_unit_used, units_done(b, v, past) - B_RING)
                nc.scalar.activation(bh[:, unit(b, v) % B_RING], zb_of(b, v), ACT.Copy).then_inc(s_b_high, 1)

            def iteration(b, past):
                n = b + AHEAD
                if n == 1:
                    act.wait_ge(s_w0_sum, 1)
                    nc.scalar.activation(w0h[:, :, :], w0s[:, :, :], ACT.Copy).then_inc(s_w0_high, 1)
                    act.wait_ge(s_wr_sum, 1)
                    nc.scalar.activation(wr_high[:, :], rs[:, :], ACT.Copy).then_inc(s_wr_high, 1)
                    relu0(0, 0)
                    act.wait_ge(s_w1_in, 16)
                    for v in range(UNITS):
                        nc.scalar.activation(w1h[:, v], w1raw[:, v, 1], ACT.Copy).then_inc(s_w1_high, 1)
                    for k, v in enumerate(A_SPLIT):
                        nc.scalar.activation(w1h[:, UNITS + k], w1raw[:, v, 0], ACT.Copy).then_inc(s_w1_high, 1)
                for name, k in ACT_ORDER:
                    if name == "A" and b >= 0:
                        high_a(b, k, past)
                    elif name == "B" and b >= 0:
                        high_b(b, k, past)
                    elif name == "square_high" and NATIVE0 <= n <= LAST:
                        square_high(n, past)
                    elif name == "xz_high" and n <= LAST:
                        xz_high(n, past)
                    elif name == "relu0" and 1 <= n - 1 <= LAST:
                        relu0(n - 1, past)
                    elif name == "sum0" and 0 <= n - 1 <= LAST:
                        sum0(n - 1, k, past)
                    elif name == "relu1" and b >= 1:
                        relu1(b - 1, past)

            blocks(act, iteration)
            relu1(LAST, 0)

        @block.vector
        def _(dve):
            nc.vector.memset(y1r[:, :], 0.0).then_inc(s_warm_zero, 1)
            nc.vector.memset(rot16[:, :, :], 1.0).then_inc(s_ones, 1)
            nc.vector.memset(w0b[0:F, 0, :], 0.0).then_inc(s_zeros, 1)
            nc.vector.memset(wr[:, :].bitcast(F32), 0.0).then_inc(s_zeros, 1)
            dve.wait_ge(s_zeros, 1)

            def first_squares(n, j):
                dve.wait_ge(s_x4_in[n], 16)
                if (n, j) == (0, 0):
                    dve.wait_ge(s_first_rot_in, 32)
                else:
                    dve.wait_ge(s_rot_in[n], rot_landed(n, 0))
                nc.vector.tensor_tensor(rot[:, n, j:j + 2], x4[:, n, :].unsqueeze(1).broadcast_to([P, 2, C]),
                                        rot[:, n, j:j + 2], ALU.mult).then_inc(s_first_squares, 1)

            first_squares(0, 0)
            dve.wait_ge(s_w0_in, 48)
            nc.vector.tensor_tensor(w0s[:, :, :], w0a, w0b, ALU.add).then_inc(s_w0_sum, 1)
            dve.wait_ge(s_wr_in, 32)
            nc.vector.tensor_tensor(rs[:, :], ra, rb, ALU.add).then_inc(s_wr_sum, 1)
            first_squares(0, 2)
            dve.wait_ge(s_w0_high, 1)
            nc.vector.tensor_tensor(w0l[:, :, :], w0s[:, :, :], w0h[:, :, :], ALU.subtract).then_inc(s_w0_low, 1)
            dve.wait_ge(s_wr_high, 1)
            nc.vector.tensor_tensor(wr_low[:, :], rs[:, :], wr_high[:, :], ALU.subtract).then_inc(s_wr_low, 1)
            dve.wait_ge(s_w1_in, 16)
            for k, v in enumerate(A_NATIVE):
                nc.vector.tensor_copy(w1n[:, k], w1raw[:, v, 0]).then_inc(s_w1_whole, 1)
            for k in range(N_SPLIT):
                dve.wait_ge(s_w1_high, k + 1)
                w = w1raw[:, k, 1] if k < UNITS else w1raw[:, A_SPLIT[k - UNITS], 0]
                nc.vector.tensor_tensor(w1l[:, k], w, w1h[:, k], ALU.subtract).then_inc(s_w1_low, 1)
            for n in range(1, SQUARES_DVE):
                first_squares(n, 0)
                first_squares(n, 2)
            dve.wait_ge(s_w1_low, N_SPLIT)
            dve.wait_ge(s_w1_whole, len(A_NATIVE))
            dve.wait_ge(s_w0_sum, 1)
            dve.wait_ge(s_wr_sum, 1)

            def form_a(b, v, past):
                u = unit(b, v)
                if v == 0:
                    dve.wait_ge(s_hid_a_in[b % 2], landed(2, b, past))
                if u >= Z_RING:
                    old_b, old_v = divmod(u - Z_RING, UNITS)
                    if old_v not in A_NATIVE:
                        dve.wait_ge(s_a_low, a_splits_done(old_b, old_v, past))
                    else:
                        dve.wait_ge(s_unit_used, units_done(old_b, old_v, past))
                dve.wait_ge(s_xb, units_done(b, v, past))
                fields = xb_of(b, v).unsqueeze(1).broadcast_to([P, 2, C])
                nc.vector.tensor_tensor(za[:, u % Z_RING], fields, hid8[:, b % HID_RING, 0:2, :],
                                        ALU.mult).then_inc(s_a, 1)

            def form_b(b, v, past):
                if v == 0:
                    dve.wait_ge(s_hid_b_in[b % 2], landed(2, b, past))
                if unit(b, v) >= ZB_RING:
                    dve.wait_ge(s_b_low, units_done(b, v, past) - ZB_RING)
                fields = xb_of(b, v).unsqueeze(1).broadcast_to([P, 2, C])
                nc.vector.tensor_tensor(zb_of(b, v), fields, hid8[:, b % HID_RING, 2:4, :],
                                        ALU.mult).then_inc(s_b, 1)

            def low_b(b, v, past):
                dve.wait_ge(s_b_high, units_done(b, v, past))
                r = unit(b, v) % B_RING
                nc.vector.tensor_tensor(bl[:, r], zb_of(b, v), bh[:, r], ALU.subtract).then_inc(s_b_low, 1)

            def sum1(b, past):
                dve.wait_ge(s_relu1, b + 1 + past)
                nc.vector.tensor_reduce(sums1[:, bass.ds(b * SB + SB * past, SB)],
                                        y1r[:, :].rearrange("p (s d) -> p s d", d=D), AX_X,
                                        ALU.add).then_inc(s_sum1, 1)

            def iteration(b, past):
                for name, v in DVE_ORDER:
                    if name == "A" and b >= 0:
                        form_a(b, v, past)
                    elif name == "B" and b >= 0:
                        form_b(b, v, past)
                    elif name == "L" and v >= 0 and b >= 0:
                        low_b(b, v, past)
                    elif name == "L" and v < 0 and b >= 1:
                        low_b(b - 1, UNITS + v, past)
                    elif name == "sum1" and b >= 1:
                        sum1(b - 1, past)

            blocks(dve, iteration)
            for name, v in DVE_ORDER:
                if name == "L" and v < 0:
                    low_b(LAST, UNITS + v, 0)
            sum1(LAST, 0)

        @block.tensor
        def _(pe):
            def layer0_native(n):
                if n == 0:
                    pe.wait_ge(s_w0_sum, 1)
                else:
                    pe.wait_ge(s_relu0, min(n, 2))
                if n >= 3:
                    pe.wait_ge(s_relu1, n - 2)
                for j in range(4):
                    if n < SQUARES_DVE:
                        pe.wait_ge(s_first_squares, 2 * n + j // 2 + 1)
                    else:
                        pe.wait_ge(s_square, squares_done(n, 0))
                    last = nc.tensor.matmul(y0_of(n), w0s[:, j, :], rot[:, n % 2, j, :], start=j == 0, stop=False)
                last.then_inc(s_square_used, 1)
                pe.wait_ge(s_xz, n + 1)
                if n == 0:
                    pe.wait_ge(s_wr_sum, 1)
                nc.tensor.matmul(y0_of(n), rs[F:F + 16, :], xz[F:F + 16, :], start=False, stop=True).then_inc(s_rest_used, 1)

            def layer0(n, past):
                if n < NATIVE0:
                    return layer0_native(n)
                if n == NATIVE0:
                    pe.wait_ge(s_w0_high, 1)
                    pe.wait_ge(s_w0_low, 1)
                pe.wait_ge(s_relu1, n - 2 + past)
                pe.wait_ge(s_square_high, splits0_done(n, past))
                for j in range(4):
                    for w in (w0h, w0l):
                        nc.tensor.matmul(y0_of(n), w[:, j, :], sqh[:, n % SQ_RING, j, :], start=j == 0 and w is w0h, stop=False)
                pe.wait_ge(s_square_low, splits0_done(n, past))
                for j in range(4):
                    last = nc.tensor.matmul(y0_of(n), w0h[:, j, :], sql[:, n % SQ_RING, j, :], start=False, stop=False)
                last.then_inc(s_square_used, 1)
                if n == NATIVE0:
                    pe.wait_ge(s_wr_put, 64)
                pe.wait_ge(s_xz_low, n + 1 + past)
                nc.tensor.matmul(y0_of(n), wr[:, :], xzs[:, n % XZ_RING, :], start=False, stop=True).then_inc(s_rest_used, 1)

            def broadcast(b, v, past):
                if (b, v) == (0, 0):
                    pe.wait_ge(s_pick, 1)
                if v == 0:
                    pe.wait_ge(s_xz_low, b + 1 + past)
                if unit(b, v) >= XB_RING:
                    pe.wait_ge(s_b, units_done(b, v, past) - XB_RING)
                nc.tensor.matmul(xb_of(b, v), pick[:, v, :], xzs[:, b % XZ_RING, :],
                                 start=True, stop=True).then_inc(s_xb, 1)

            def split_terms(b, tiles, s_high, s_low, value, k_w, high, low, start, stop):
                pe.wait_ge(s_high, value)
                for k in range(tiles):
                    for w in (w1h, w1l):
                        nc.tensor.matmul(y1_of(b), w[:, k_w, k, :], high[:, k, :],
                                         start=start and k == 0 and w is w1h, stop=False)
                pe.wait_ge(s_low, value)
                for k in range(tiles):
                    last = nc.tensor.matmul(y1_of(b), w1h[:, k_w, k, :], low[:, k, :],
                                            start=False, stop=stop and k == tiles - 1)
                return last

            def contract_a(b, v, past):
                if v == 0 and 1 <= b < LAST:
                    pe.wait_ge(s_relu0, b + 2 + past)
                elif v == 0 and b == LAST:
                    pe.wait_ge(s_relu1, b - 1)
                if (b, v) == (0, 0):
                    pe.wait_ge(s_w1_low, N_SPLIT)
                    pe.wait_ge(s_w1_whole, len(A_NATIVE))
                tiles = A_TILES_SPLIT.get(v, 0)
                if tiles < 2:
                    pe.wait_ge(s_a, units_done(b, v, past))
                for k in range(tiles, 2):
                    nc.tensor.matmul(y1_of(b), w1n[:, A_NATIVE.index(v), k, :], za[:, unit(b, v) % Z_RING, k, :],
                                     start=v == 0 and k == tiles, stop=False)
                if tiles:
                    r = (a_splits_done(b, v, 0) - 1) % A_RING
                    split_terms(b, tiles, s_a_high, s_a_low, a_splits_done(b, v, past), UNITS + A_SPLIT.index(v),
                                ah[:, r], al[:, r], v == 0 and tiles == 2, False)

            def contract_b(b, v, past):
                r = unit(b, v) % B_RING
                split_terms(b, 2, s_b_high, s_b_low, units_done(b, v, past), v, bh[:, r], bl[:, r],
                            False, v == UNITS - 1).then_inc(s_unit_used, 1)

            def iteration(b, past):
                for name, v in PE_ORDER_FIRST if b == 0 else PE_ORDER:
                    ahead_b, ahead_v = divmod(unit(b, v) + XB_LEAD, UNITS)
                    if name == "layer0" and b + AHEAD != 1 and b + AHEAD <= LAST:
                        layer0(b + AHEAD, past)
                    elif name == "layer0 of 1":
                        layer0(1, 0)
                    elif name == "X" and 0 <= ahead_b <= LAST:
                        broadcast(ahead_b, ahead_v, past)
                    elif name == "A" and b >= 0:
                        contract_a(b, v, past)
                    elif name == "B" and b >= 0:
                        contract_b(b, v, past)

            pe.wait_ge(s_warm_zero, 1)
            for _ in range(WARM_UP):
                nc.tensor.matmul(y0_of(0), y1r[:, 0:P], y1r[:, :], start=True, stop=True)

            blocks(pe, iteration)


def kernel(r_cin_inputs, L0_rec_w0, L0_rec_b0, L0_rec_w1, L0_rec_b1):
    import numpy as np
    import concourse.bacc as bacc
    from concourse.bass_utils import run_bass_kernel_spmd

    x = np.asarray(r_cin_inputs)
    B, F_, D_ = x.shape
    x = x.transpose(1, 0, 2).reshape(F_, B * D_)
    x_rows = np.ascontiguousarray(np.concatenate([x, x[:16]], axis=0))
    w0 = np.asarray(L0_rec_w0).T.reshape(F_, F_, -1)
    i = np.arange(F_)
    near = np.stack([w0[i, (i + k) % F_] for k in range(17)]).reshape(17 * F_, -1)
    far = np.stack([w0[(i + k) % F_, i] for k in range(17)]).reshape(17 * F_, -1)
    w1 = np.asarray(L0_rec_w1).T.reshape(4, 16, 4, 8, -1).transpose(1, 3, 2, 0, 4).reshape(128, -1)
    arrays = {
        "x_rows": x_rows,
        "w0_near": np.ascontiguousarray(near),
        "w0_far": np.ascontiguousarray(far),
        "w1_tiles": np.ascontiguousarray(w1),
        "b0": np.ascontiguousarray(np.asarray(L0_rec_b0).reshape(-1, 1)),
        "b1": np.ascontiguousarray(np.asarray(L0_rec_b1).reshape(-1, 1)),
    }
    nc = bacc.Bacc("TRN2", target_bir_lowering=False, num_devices=1)
    args = [nc.dram_tensor(name, a.shape, mybir.dt.from_np(a.dtype), kind="ExternalInput").ap()
            for name, a in arrays.items()]
    args.append(nc.dram_tensor("out", (192, B), F32, kind="ExternalOutput").ap())
    cin_kernel(nc, *args)
    r = run_bass_kernel_spmd(nc, [arrays], core_ids=[0])
    return np.ascontiguousarray(r.results[0]["out"].T)
```
